# Optimizing a Trainium2 kernel written in Bass

```python
import numpy as np
import jax
import jax.numpy as jnp

def _softmax(x, axis=-1):
    return jax.nn.softmax(x, axis=axis)

def _gelu(x):
    return jax.nn.gelu(x, approximate=True)

def _silu(x):
    return jax.nn.silu(x)

def _sigmoid(x):
    return jax.nn.sigmoid(x)

def _layernorm(x, axis=-1, eps=1e-05):
    m = jnp.mean(x, axis=axis, keepdims=True)
    v = jnp.var(x, axis=axis, keepdims=True)
    return (x - m) / jnp.sqrt(v + eps)

def _scatter_add(tgt, idx, src, axis=0):
    return tgt.at[idx].add(src)

def _segment_sum(src, seg, n):
    return jax.ops.segment_sum(src, seg, n)
kernel_name = 'mk_cond_resid_d2_seqx_r2_609f6d'

def setup_inputs(seed: int=0):
    np.random.seed(seed)
    _w = jnp.asarray

    def _rec_inputs():
        import jax
        import jax.numpy as jnp
        _rk = jax.random.key(seed)
        x = -0.000125 + 0.9999 * jax.random.normal(jax.random.fold_in(_rk, 1), (2, 2048, 512), jnp.float32)
        _lenS = 2048 - jax.random.randint(jax.random.fold_in(_rk, 7), (2,), 0, max(1, 2048 // 4) + 1, jnp.int32)
        _lenS2 = 2048 - jax.random.randint(jax.random.fold_in(_rk, 8), (2,), 0, max(1, 2048 // 4) + 1, jnp.int32)
        cond_1024 = -0.00493535 + 1.00056 * jax.random.normal(jax.random.fold_in(_rk, 11), (2, 512), jnp.float32)
        return (x, cond_1024)
    x, cond_1024 = _rec_inputs()

    def _L0_cond_setup():
        import jax, jax.numpy as jnp
        import numpy as np
        N, T, D, H = (64, 256, 512, 512)
        key = jax.random.key(seed)
        k1, k2, k3, k4 = jax.random.split(key, 4)
        x = jax.random.normal(k1, (N, T, D), dtype=jnp.float32)
        h0 = jax.random.normal(k2, (N, H), dtype=jnp.float32)
        Wx = jax.random.normal(k3, (D, H), dtype=jnp.float32) / np.sqrt(D)
        Wh = jax.random.normal(k4, (H, H), dtype=jnp.float32) / np.sqrt(H)
        b = jnp.zeros((H,), dtype=jnp.float32)
        return {'x': x, 'h0': h0, 'Wx': Wx, 'Wh': Wh, 'b': b}
    _L0_cond_all = _L0_cond_setup()
    _L0_cond_in = {k: v for k, v in _L0_cond_all.items() if k in ('Wx', 'Wh', 'b')}
    del _L0_cond_all

    def _L1_cond_setup():
        import jax, jax.numpy as jnp
        import numpy as np
        N, T, D, H = (64, 256, 512, 512)
        key = jax.random.key(seed)
        k1, k2, k3, k4 = jax.random.split(key, 4)
        x = jax.random.normal(k1, (N, T, D), dtype=jnp.float32)
        h0 = jax.random.normal(k2, (N, H), dtype=jnp.float32)
        Wx = jax.random.normal(k3, (D, H), dtype=jnp.float32) / np.sqrt(D)
        Wh = jax.random.normal(k4, (H, H), dtype=jnp.float32) / np.sqrt(H)
        b = jnp.zeros((H,), dtype=jnp.float32)
        return {'x': x, 'h0': h0, 'Wx': Wx, 'Wh': Wh, 'b': b}
    _L1_cond_all = _L1_cond_setup()
    _L1_cond_in = {k: v for k, v in _L1_cond_all.items() if k in ('Wx', 'Wh', 'b')}
    del _L1_cond_all
    return {'x': x, 'cond_1024': cond_1024, 'L0_cond_Wx': _L0_cond_in['Wx'], 'L0_cond_Wh': _L0_cond_in['Wh'], 'L0_cond_b': _L0_cond_in['b'], 'L1_cond_Wx': _L1_cond_in['Wx'], 'L1_cond_Wh': _L1_cond_in['Wh'], 'L1_cond_b': _L1_cond_in['b']}

def reference(x, cond_1024, L0_cond_Wx, L0_cond_Wh, L0_cond_b, L1_cond_Wx, L1_cond_Wh, L1_cond_b):
    import jax
    import jax.numpy as jnp

    def _L0_cond_ref(x, h0, Wx, Wh, b):
        import jax, jax.numpy as jnp
        import numpy as np
        N, T, D, H = (64, 256, 512, 512)
        xW = jnp.einsum('ntd,dh->nth', x, Wx) + b
        xW_t = jnp.swapaxes(xW, 0, 1)

        def step(prev_h, xw):
            next_h = jnp.tanh(prev_h @ Wh + xw)
            return (next_h, next_h)
        _, h_t = jax.lax.scan(step, h0, xW_t)
        return jnp.swapaxes(h_t, 0, 1)

    def _L1_cond_ref(x, h0, Wx, Wh, b):
        import jax, jax.numpy as jnp
        import numpy as np
        N, T, D, H = (64, 256, 512, 512)
        xw = jnp.einsum('ntd,dh->nth', x, Wx) + b

        def step(prev_h, xw_t):
            next_h = jnp.tanh(prev_h @ Wh + xw_t)
            return (next_h, next_h)
        _, hs = jax.lax.scan(step, h0, jnp.swapaxes(xw, 0, 1))
        return jnp.swapaxes(hs, 0, 1)
    x = x + _L0_cond_ref(x, cond_1024, L0_cond_Wx, L0_cond_Wh, L0_cond_b)
    x = x + _L1_cond_ref(x, cond_1024, L1_cond_Wx, L1_cond_Wh, L1_cond_b)
    return x

_drawn_inputs = setup_inputs


def setup_inputs(seed=0):
    import zlib

    import numpy as np

    out = dict(_drawn_inputs(seed))
    spreads = {'L0_cond_b': (0.0, 0.1), 'L1_cond_b': (0.0, 0.1)}
    factors = {'cond_1024': 3.199}
    for name, (base, spread) in spreads.items():
        noise = np.random.default_rng([zlib.crc32(name.encode()), seed]).standard_normal(out[name].shape)
        drawn = base * np.exp(spread * noise) if base else spread * noise
        out[name] = jnp.asarray(drawn.astype(out[name].dtype))
    for name, factor in factors.items():
        out[name] = (out[name] * factor).astype(out[name].dtype)
    return out
```

```python
import concourse.bass as bass
from concourse import mybir
from contextlib import ExitStack


def residual_rnn_pair(nc, x_t, cond_t, wx0, wh0, b0, wx1, wh1, b1, out_t):
    fp32 = mybir.dt.float32
    fp16 = mybir.dt.float16
    ALU = mybir.AluOpType
    ACT = mybir.ActivationFunctionType
    AX = mybir.AxisListType

    P = 128
    D = wx0.shape[0]
    M = D // P
    B = cond_t.shape[1] // M
    U = 8
    CW = M * U * B
    C = x_t.shape[1] // CW
    S = 2
    HI, LO = 0, 1
    H = 2
    MH = M // H
    L = (0, 1)
    WSCALE = 4096.0
    BPARTS = 3

    STORES = [64, 64, 64, 32, 16, 8, 4, 3, 1]
    assert sum(STORES) == C
    B_STEPS = len(L) * (3 * BPARTS - 1)

    wx, wh, bias = (wx0, wx1), (wh0, wh1), (b0, b1)

    with ExitStack() as ctx:
        def sb(name, shape, dt):
            return ctx.enter_context(nc.sbuf_tensor(name, shape, dt))

        def sem(name):
            return ctx.enter_context(nc.semaphore(name))

        def per_layer(make, name, *args):
            return [make(f"{name}{l}", *args) for l in L]

        X = sb("X", [P, C * CW], fp32)
        cond = sb("cond", [P, M * B], fp32)
        w_f32 = {(kind, l): sb(f"w_f32_{kind}{l}", [P, M, D], fp32) for l in L for kind in ("x", "h")}
        w_part = {(kind, l): sb(f"w_part_{kind}{l}", [P, M, S, D], fp16) for l in L for kind in ("x", "h")}
        b_f32 = per_layer(sb, "b_f32_", [P, P], fp32)
        b_rest = per_layer(sb, "b_rest_", [P, P], fp32)
        b_tmp = per_layer(sb, "b_tmp_", [P, P], fp16)
        b_part = per_layer(sb, "b_part_", [P, P], fp16)
        b_select = sb("b_select", [P, M, U * B], fp16)
        x_part = per_layer(sb, "x_part_", [P, M, S, U * B], fp16)
        h_part = per_layer(sb, "h_part_", [P, M, S, B], fp16)
        h_chunk = per_layer(sb, "h_chunk_", [P, M, U, B], fp32)
        z_sum = per_layer(sb, "z_sum_", [P, M, B], fp32)
        Z = [[ctx.enter_context(nc.psum_tensor(f"Z{l}_{h}", [P, 512], fp32)) for h in range(H)] for l in L]
        z_chunk = [[z[:, 0:MH * S * U * B].rearrange("p (m s u b) -> p m s u b", m=MH, s=S, u=U) for z in zs]
                   for zs in Z]

        cond_loaded = sem("cond_loaded")
        x_first_loaded = sem("x_first_loaded")
        x_rest_loaded = sem("x_rest_loaded")
        b_loaded = per_layer(sem, "b_loaded_")
        wx_loaded = per_layer(sem, "wx_loaded_")
        wh_loaded = per_layer(sem, "wh_loaded_")
        b_zeroed = sem("b_zeroed")
        select_step = sem("select_step")
        wx_hi = per_layer(sem, "wx_hi_")
        wh_hi = per_layer(sem, "wh_hi_")
        wx_ready = per_layer(sem, "wx_ready_")
        wh_ready = per_layer(sem, "wh_ready_")
        b_step = sem("b_step")
        h0_hi = sem("h0_hi")
        x_hi = per_layer(sem, "x_hi_")
        x_ready = per_layer(sem, "x_ready_")
        proj_done = per_layer(sem, "proj_done_")
        z_ready = per_layer(sem, "z_ready_")
        sum_ready = per_layer(sem, "sum_ready_")
        tanh_done = per_layer(sem, "tanh_done_")
        h_ready = per_layer(sem, "h_ready_")
        h_used = per_layer(sem, "h_used_")
        pool_waited = sem("pool_waited")
        stored = sem("stored")

        def half(h):
            return slice(h * MH, (h + 1) * MH)

        def halves(c, u, h):
            return c * (H * U) + (H * u + h + 1)

        block = ctx.enter_context(nc.Block())
        FIRST = 2 * CW

        @block.sync
        def _(sp):
            sp.dma_start(cond[:, :], cond_t).then_inc(cond_loaded, 16)
            sp.dma_start(X[:, 0:FIRST], x_t[:, 0:FIRST]).then_inc(x_first_loaded, 16)
            sp.wait_ge(b_zeroed, 1)
            for l in L:
                for part in range(BPARTS):
                    sp.dma_start(b_f32[l][32 * part:32 * part + M, :],
                                 bias[l].rearrange("(m p) -> m p", p=P)).then_inc(b_loaded[l], 16)
            sp.dma_start(w_f32["x", 0][:, :, :], wx0.rearrange("(k p) n -> p k n", p=P)).then_inc(wx_loaded[0], 16)
            sp.dma_start(w_f32["h", 0][:, :, :], wh0.rearrange("(k p) n -> p k n", p=P)).then_inc(wh_loaded[0], 16)
            sp.dma_start(w_f32["x", 1][:, :, :], wx1.rearrange("(k p) n -> p k n", p=P)).then_inc(wx_loaded[1], 16)
            sp.dma_start(w_f32["h", 1][:, :, :], wh1.rearrange("(k p) n -> p k n", p=P)).then_inc(wh_loaded[1], 16)
            sp.dma_start(X[:, FIRST:], x_t[:, FIRST:]).then_inc(x_rest_loaded, 16)
            c = 0
            for n in STORES:
                sp.wait_ge(h_used[1], c + n)
                sp.dma_start(out_t[:, c * CW:(c + n) * CW], X[:, c * CW:(c + n) * CW]).then_inc(stored, 16)
                c += n
            sp.wait_ge(stored, 16 * len(STORES))

        @block.gpsimd
        def _(pool):
            nc.gpsimd.memset(b_select[:, :, :], 0.0).then_inc(select_step, 1)
            for part in range(BPARTS):
                pool.wait_ge(select_step, part + 1)
                nc.gpsimd.affine_select(out=b_select[:, :, :], in_=b_select[:, :, :], compare_op=ALU.not_equal,
                                        fill=WSCALE, base=-32 * part, pattern=[[-1, M], [0, U * B]],
                                        channel_multiplier=1).then_inc(select_step, 1)

            def chunk(c):
                return X[:, bass.ds(c * CW, CW)].rearrange("p (m n) -> p m n", m=M)

            def wait_apart(what, value):
                pool.wait_ge(what, value)
                pool.sem_inc(pool_waited, 1)

            def split_x(l, c):
                nc.gpsimd.tensor_copy(x_part[l][:, :, HI, :], chunk(c)).then_inc(x_hi[l], 1)
                wait_apart(x_hi[l], c + 1)
                nc.gpsimd.tensor_tensor(x_part[l][:, :, LO, :], chunk(c), x_part[l][:, :, HI, :],
                                        ALU.subtract).then_inc(x_ready[l], 1)

            def add_states(l, c):
                nc.gpsimd.tensor_tensor(chunk(c), chunk(c), h_chunk[l][:, :, :, :].rearrange("p m u b -> p m (u b)"),
                                        ALU.add).then_inc(h_used[l], 1)

            def turn(c, split0=True, layer0=True, layer1=True):
                if split0:
                    wait_apart(proj_done[0], c + 1)
                    split_x(0, c + 1)
                if layer0:
                    wait_apart(tanh_done[0], c * (H * U) + H * U)
                    add_states(0, c)
                    if not isinstance(c, int) or c >= 1:
                        wait_apart(proj_done[1], c)
                    wait_apart(h_used[0], c + 1)
                    split_x(1, c)
                if layer1:
                    wait_apart(tanh_done[1], c * (H * U))
                    add_states(1, c - 1)

            pool.wait_ge(x_first_loaded, 16)
            split_x(0, 0)
            turn(0, layer1=False)
            pool.wait_ge(x_rest_loaded, 16)
            with pool.Fori(1, C - 1) as c:
                turn(c)
            turn(C - 1, split0=False)
            turn(C, split0=False, layer0=False)

        @block.scalar
        def _(act):
            for l in L:
                for kind, loaded, done in (("x", wx_loaded, wx_hi), ("h", wh_loaded, wh_hi)):
                    act.wait_ge(loaded[l], 16)
                    nc.scalar.activation(w_part[kind, l][:, :, HI, :], w_f32[kind, l][:, :, :], ACT.Copy,
                                         scale=WSCALE).then_inc(done[l], 1)

            def step(l, c, u):
                if u == 0 and (not isinstance(c, int) or c >= 1):
                    act.wait_ge(h_used[l], c)
                for h in range(H):
                    act.wait_ge(sum_ready[l], halves(c, u, h))
                    nc.scalar.activation(h_part[l][:, half(h), HI, :], z_sum[l][:, half(h), :], ACT.Tanh,
                                         scale=1.0 / WSCALE)
                    nc.scalar.activation(h_chunk[l][:, half(h), u, :], z_sum[l][:, half(h), :], ACT.Tanh,
                                         scale=1.0 / WSCALE).then_inc(tanh_done[l], 1)

            for u in range(U):
                step(0, 0, u)
            with act.Fori(1, C) as c:
                for u in range(U):
                    step(0, c, u)
                    step(1, c - 1, u)
            for u in range(U):
                step(1, C - 1, u)

        @block.vector
        def _(dve):
            for l in L:
                nc.vector.memset(b_f32[l][:, :], 0.0)
                last = nc.vector.memset(b_part[l][:, :], 0.0)
            last.then_inc(b_zeroed, 1)

            dve.wait_ge(cond_loaded, 16)
            start = cond[:, :].rearrange("p (m b) -> p m b", m=M)
            for l in L:
                nc.vector.tensor_copy(h_part[l][:, :, HI, :], start).then_inc(h0_hi, 1)
            for l in L:
                dve.wait_ge(h0_hi, l + 1)
                for h in range(H):
                    nc.vector.tensor_tensor(h_part[l][:, half(h), LO, :], start[:, half(h), :],
                                            h_part[l][:, half(h), HI, :], ALU.subtract).then_inc(h_ready[l], 1)

            bs = 0
            for l in L:
                dve.wait_ge(b_loaded[l], 16 * BPARTS)
                rest = b_f32[l]
                for part in range(BPARTS):
                    nc.vector.tensor_copy(b_tmp[l][:, :], rest[:, :]).then_inc(b_step, 1)
                    bs += 1
                    dve.wait_ge(b_step, bs)
                    rows = slice(32 * part, 32 * part + M)
                    nc.vector.tensor_copy(b_part[l][rows, :], b_tmp[l][rows, :]).then_inc(b_step, 1)
                    bs += 1
                    if part < BPARTS - 1:
                        nc.vector.tensor_tensor(b_rest[l][:, :], rest[:, :], b_tmp[l][:, :],
                                                ALU.subtract).then_inc(b_step, 1)
                        bs += 1
                        dve.wait_ge(b_step, bs)
                        rest = b_rest[l]
            assert bs == B_STEPS

            for l in L:
                for kind, hi, done in (("x", wx_hi, wx_ready), ("h", wh_hi, wh_ready)):
                    dve.wait_ge(hi[l], 1)
                    nc.vector.scalar_tensor_tensor(
                        out=w_part[kind, l][:, :, LO, :], in0=w_f32[kind, l][:, :, :], scalar=WSCALE,
                        in1=w_part[kind, l][:, :, HI, :], op0=ALU.mult, op1=ALU.subtract).then_inc(done[l], 1)

            def step(l, c, u):
                for h in range(H):
                    dve.wait_ge(z_ready[l], halves(c, u, h))
                    nc.vector.tensor_reduce(z_sum[l][:, half(h), :],
                                            z_chunk[l][h][:, :, :, u, :].rearrange("p m s b -> p m b s"),
                                            AX.X, ALU.add).then_inc(sum_ready[l], 1)
                for h in range(H):
                    dve.wait_ge(tanh_done[l], halves(c, u, h))
                    nc.vector.tensor_tensor(h_part[l][:, half(h), LO, :], h_chunk[l][:, half(h), u, :],
                                            h_part[l][:, half(h), HI, :], ALU.subtract).then_inc(h_ready[l], 1)

            for u in range(U):
                step(0, 0, u)
            with dve.Fori(1, C) as c:
                for u in range(U):
                    step(0, c, u)
                    step(1, c - 1, u)
            for u in range(U):
                step(1, C - 1, u)

        @block.tensor
        def _(pe):
            def project(l, c):
                pe.wait_ge(x_ready[l], c + 1)
                pe.wait_ge(h_ready[l], c * (H * U) + H)
                for h in range(H):
                    nc.tensor.matmul(z_chunk[l][h][:, :, HI, :, :].rearrange("p m u b -> p m (u b)"),
                                     b_part[l][:, :], b_select[:, half(h), :],
                                     start=True, stop=False, skip_group_check=True)
                    for m in range(MH):
                        mm = h * MH + m
                        for k in range(M):
                            for w in range(S):
                                last = nc.tensor.matmul(
                                    Z[l][h][:, m * S * U * B:(m + 1) * S * U * B],
                                    w_part["x", l][:, k, w, mm * P:(mm + 1) * P],
                                    x_part[l][:, k, :, :].rearrange("p s n -> p (s n)"),
                                    start=False, stop=False, skip_group_check=True)
                last.then_inc(proj_done[l], 1)

            def step(l, c, u):
                for hk in range(H):
                    for h in range(H):
                        if hk == 0:
                            pe.wait_ge(h_ready[l], halves(c, u, h))
                        for m in range(MH):
                            mm = h * MH + m
                            for k in range(hk * MH, (hk + 1) * MH):
                                for w in range(S):
                                    last = nc.tensor.matmul(
                                        z_chunk[l][h][:, m, :, u, :], w_part["h", l][:, k, w, mm * P:(mm + 1) * P],
                                        h_part[l][:, k, :, :], start=False, stop=True, skip_group_check=True)
                        if hk == H - 1:
                            last.then_inc(z_ready[l], 1)

            pe.wait_ge(select_step, 1 + BPARTS)
            pe.wait_ge(b_step, B_STEPS)
            pe.wait_ge(wx_ready[0], 1)
            project(0, 0)
            pe.wait_ge(wh_ready[0], 1)
            for u in range(U):
                step(0, 0, u)
            pe.wait_ge(wx_ready[1], 1)
            pe.wait_ge(wh_ready[1], 1)
            with pe.Fori(1, C) as c:
                project(0, c)
                step(0, c, 0)
                project(1, c - 1)
                step(1, c - 1, 0)
                for u in range(1, U):
                    step(0, c, u)
                    step(1, c - 1, u)
            project(1, C - 1)
            for u in range(U):
                step(1, C - 1, u)


def kernel(x, cond_1024, L0_cond_Wx, L0_cond_Wh, L0_cond_b, L1_cond_Wx, L1_cond_Wh, L1_cond_b):
    import numpy as np
    import concourse.bacc as bacc
    from concourse.bass_utils import run_bass_kernel_spmd

    P, U = 128, 8
    x, cond = np.asarray(x), np.asarray(cond_1024)
    B, T, D = x.shape
    M, C = D // P, T // U
    x_t = x.reshape(B, C, U, M, P).transpose(4, 1, 3, 2, 0).reshape(P, -1)
    cond_t = cond.reshape(B, M, P).transpose(2, 1, 0).reshape(P, -1)
    arrays = {"x_t": x_t, "cond_t": cond_t, "wx0": L0_cond_Wx, "wh0": L0_cond_Wh, "b0": L0_cond_b,
              "wx1": L1_cond_Wx, "wh1": L1_cond_Wh, "b1": L1_cond_b}
    arrays = {name: np.ascontiguousarray(a) for name, a in arrays.items()}

    nc = bacc.Bacc("TRN2", target_bir_lowering=False, num_devices=1)
    ins = [nc.dram_tensor(name, a.shape, mybir.dt.from_np(a.dtype), kind="ExternalInput").ap()
           for name, a in arrays.items()]
    out_t = nc.dram_tensor("out_t", x_t.shape, mybir.dt.float32, kind="ExternalOutput").ap()
    residual_rnn_pair(nc, *ins, out_t)
    r = run_bass_kernel_spmd(nc, [arrays], core_ids=[0])
    got = r.results[0]["out_t"]
    return np.ascontiguousarray(got.reshape(P, C, M, U, B).transpose(4, 1, 3, 2, 0).reshape(B, T, D))
```

```python
import concourse.bass as bass
from concourse import mybir
from contextlib import ExitStack


def residual_rnn_pair(nc, x_t, cond_t, wx0, wh0, b0, wx1, wh1, b1, out_t):
    fp32 = mybir.dt.float32
    fp16 = mybir.dt.float16
    ALU = mybir.AluOpType
    ACT = mybir.ActivationFunctionType
    AX = mybir.AxisListType

    P = 128
    D = wx0.shape[0]
    M = D // P
    B = cond_t.shape[1] // M
    U = 16
    CW = M * U * B
    C = x_t.shape[1] // CW
    S = 2
    HI, LO = 0, 1
    NW = 32
    H = 2
    MH = M // H
    L = (0, 1)
    WSCALE = 4096.0
    BPARTS = 3

    STORES = [32, 32, 32, 16, 8, 4, 2, 1, 1]
    assert sum(STORES) == C
    B_STEPS = len(L) * (3 * BPARTS - 1)

    wx, wh, bias = (wx0, wx1), (wh0, wh1), (b0, b1)

    with ExitStack() as ctx:
        def sb(name, shape, dt):
            return ctx.enter_context(nc.sbuf_tensor(name, shape, dt))

        def sem(name):
            return ctx.enter_context(nc.semaphore(name))

        def per_layer(make, name, *args):
            return [make(f"{name}{l}", *args) for l in L]

        X = sb("X", [P, C * CW], fp32)
        cond = sb("cond", [P, M * B], fp32)
        w_f32 = {(kind, l): sb(f"w_f32_{kind}{l}", [P, M, D], fp32) for l in L for kind in ("x", "h")}
        w_part = {(kind, l): sb(f"w_part_{kind}{l}", [P, M, S, D], fp16) for l in L for kind in ("x", "h")}
        b_f32 = per_layer(sb, "b_f32_", [P, P], fp32)
        b_rest = per_layer(sb, "b_rest_", [P, P], fp32)
        b_tmp = per_layer(sb, "b_tmp_", [P, P], fp16)
        b_part = per_layer(sb, "b_part_", [P, P], fp16)
        b_select = sb("b_select", [P, M, U, B], fp16)
        x_part = per_layer(sb, "x_part_", [P, M, U, S, B], fp16)
        h_wide = per_layer(sb, "h_wide_", [P, M, NW], fp16)
        h_part = [h[:, :, 0:S * B].rearrange("p m (s b) -> p m s b", s=S) for h in h_wide]
        h_chunk = per_layer(sb, "h_chunk_", [P, M, U, B], fp32)
        z_sum = per_layer(sb, "z_sum_", [P, M, B], fp32)
        Z = [[ctx.enter_context(nc.psum_tensor(f"Z{l}_{h}", [P, 512], fp32)) for h in range(H)] for l in L]
        z_chunk = [[z[:, 0:MH * U * S * B].rearrange("p (m u s b) -> p m u s b", m=MH, u=U, s=S) for z in zs]
                   for zs in Z]

        cond_loaded = sem("cond_loaded")
        x_first_loaded = sem("x_first_loaded")
        x_rest_loaded = sem("x_rest_loaded")
        b_loaded = per_layer(sem, "b_loaded_")
        wx_loaded = per_layer(sem, "wx_loaded_")
        wh_loaded = per_layer(sem, "wh_loaded_")
        zeroed = sem("zeroed")
        select_step = sem("select_step")
        wx_hi = per_layer(sem, "wx_hi_")
        wh_hi = per_layer(sem, "wh_hi_")
        wx_ready = per_layer(sem, "wx_ready_")
        wh_ready = per_layer(sem, "wh_ready_")
        b_step = sem("b_step")
        h0_hi = sem("h0_hi")
        x_hi = per_layer(sem, "x_hi_")
        x_ready = per_layer(sem, "x_ready_")
        proj_done = per_layer(sem, "proj_done_")
        z_ready = per_layer(sem, "z_ready_")
        sum_ready = per_layer(sem, "sum_ready_")
        tanh_done = per_layer(sem, "tanh_done_")
        h_ready = per_layer(sem, "h_ready_")
        h_used = per_layer(sem, "h_used_")
        pool_waited = sem("pool_waited")
        stored = sem("stored")

        def half(h):
            return slice(h * MH, (h + 1) * MH)

        def halves(c, u, h):
            return c * (H * U) + (H * u + h + 1)

        block = ctx.enter_context(nc.Block())
        FIRST = 2 * CW

        @block.sync
        def _(sp):
            sp.dma_start(cond[:, :], cond_t).then_inc(cond_loaded, 16)
            sp.dma_start(X[:, 0:FIRST], x_t[:, 0:FIRST]).then_inc(x_first_loaded, 16)
            sp.wait_ge(zeroed, 1)
            for l in L:
                for part in range(BPARTS):
                    sp.dma_start(b_f32[l][32 * part:32 * part + M, :],
                                 bias[l].rearrange("(m p) -> m p", p=P)).then_inc(b_loaded[l], 16)
            sp.dma_start(w_f32["x", 0][:, :, :], wx0.rearrange("(k p) n -> p k n", p=P)).then_inc(wx_loaded[0], 16)
            sp.dma_start(w_f32["h", 0][:, :, :], wh0.rearrange("(k p) n -> p k n", p=P)).then_inc(wh_loaded[0], 16)
            sp.dma_start(w_f32["x", 1][:, :, :], wx1.rearrange("(k p) n -> p k n", p=P)).then_inc(wx_loaded[1], 16)
            sp.dma_start(w_f32["h", 1][:, :, :], wh1.rearrange("(k p) n -> p k n", p=P)).then_inc(wh_loaded[1], 16)
            sp.dma_start(X[:, FIRST:], x_t[:, FIRST:]).then_inc(x_rest_loaded, 16)
            c = 0
            for n in STORES:
                sp.wait_ge(h_used[1], c + n)
                sp.dma_start(out_t[:, c * CW:(c + n) * CW], X[:, c * CW:(c + n) * CW]).then_inc(stored, 16)
                c += n
            sp.wait_ge(stored, 16 * len(STORES))

        @block.gpsimd
        def _(pool):
            nc.gpsimd.memset(b_select[:, :, :, :], 0.0).then_inc(select_step, 1)
            for part in range(BPARTS):
                pool.wait_ge(select_step, part + 1)
                nc.gpsimd.affine_select(out=b_select[:, :, :, :], in_=b_select[:, :, :, :], compare_op=ALU.not_equal,
                                        fill=WSCALE, base=-32 * part, pattern=[[-1, M], [0, U], [0, B]],
                                        channel_multiplier=1).then_inc(select_step, 1)

            def chunk(c):
                return X[:, bass.ds(c * CW, CW)].rearrange("p (m u b) -> p m u b", m=M, u=U)

            def wait_apart(what, value):
                pool.wait_ge(what, value)
                pool.sem_inc(pool_waited, 1)

            def split_x(l, c):
                nc.gpsimd.tensor_copy(x_part[l][:, :, :, HI, :], chunk(c)).then_inc(x_hi[l], 1)
                wait_apart(x_hi[l], c + 1)
                nc.gpsimd.tensor_tensor(x_part[l][:, :, :, LO, :], chunk(c), x_part[l][:, :, :, HI, :],
                                        ALU.subtract).then_inc(x_ready[l], 1)

            def add_states(l, c):
                nc.gpsimd.tensor_tensor(chunk(c), chunk(c), h_chunk[l][:, :, :, :], ALU.add).then_inc(h_used[l], 1)

            def turn(c, split0=True, layer0=True, layer1=True):
                if split0:
                    wait_apart(proj_done[0], c + 1)
                    split_x(0, c + 1)
                if layer0:
                    wait_apart(tanh_done[0], c * (H * U) + H * U)
                    add_states(0, c)
                    if not isinstance(c, int) or c >= 1:
                        wait_apart(proj_done[1], c)
                    wait_apart(h_used[0], c + 1)
                    split_x(1, c)
                if layer1:
                    wait_apart(tanh_done[1], c * (H * U))
                    add_states(1, c - 1)

            pool.wait_ge(x_first_loaded, 16)
            split_x(0, 0)
            turn(0, layer1=False)
            pool.wait_ge(x_rest_loaded, 16)
            with pool.Fori(1, C - 1) as c:
                turn(c)
            turn(C - 1, split0=False)
            turn(C, split0=False, layer0=False)

        @block.scalar
        def _(act):
            for l in L:
                for kind, loaded, done in (("x", wx_loaded, wx_hi), ("h", wh_loaded, wh_hi)):
                    act.wait_ge(loaded[l], 16)
                    nc.scalar.activation(w_part[kind, l][:, :, HI, :], w_f32[kind, l][:, :, :], ACT.Copy,
                                         scale=WSCALE).then_inc(done[l], 1)

            def step(l, c, u):
                if u == 0 and (not isinstance(c, int) or c >= 1):
                    act.wait_ge(h_used[l], c)
                for h in range(H):
                    act.wait_ge(sum_ready[l], halves(c, u, h))
                    nc.scalar.activation(h_part[l][:, half(h), HI, :], z_sum[l][:, half(h), :], ACT.Tanh,
                                         scale=1.0 / WSCALE)
                    nc.scalar.activation(h_chunk[l][:, half(h), u, :], z_sum[l][:, half(h), :], ACT.Tanh,
                                         scale=1.0 / WSCALE).then_inc(tanh_done[l], 1)

            for u in range(U):
                step(0, 0, u)
            with act.Fori(1, C) as c:
                for u in range(U):
                    step(0, c, u)
                    step(1, c - 1, u)
            for u in range(U):
                step(1, C - 1, u)

        @block.vector
        def _(dve):
            for l in L:
                nc.vector.memset(b_f32[l][:, :], 0.0)
                nc.vector.memset(b_part[l][:, :], 0.0)
                last = nc.vector.memset(h_wide[l][:, :, :], 0.0)
            last.then_inc(zeroed, 1)

            dve.wait_ge(cond_loaded, 16)
            dve.wait_ge(zeroed, 1)
            start = cond[:, :].rearrange("p (m b) -> p m b", m=M)
            for l in L:
                nc.vector.tensor_copy(h_part[l][:, :, HI, :], start).then_inc(h0_hi, 1)
            for l in L:
                dve.wait_ge(h0_hi, l + 1)
                for h in range(H):
                    nc.vector.tensor_tensor(h_part[l][:, half(h), LO, :], start[:, half(h), :],
                                            h_part[l][:, half(h), HI, :], ALU.subtract).then_inc(h_ready[l], 1)

            bs = 0
            for l in L:
                dve.wait_ge(b_loaded[l], 16 * BPARTS)
                rest = b_f32[l]
                for part in range(BPARTS):
                    nc.vector.tensor_copy(b_tmp[l][:, :], rest[:, :]).then_inc(b_step, 1)
                    bs += 1
                    dve.wait_ge(b_step, bs)
                    rows = slice(32 * part, 32 * part + M)
                    nc.vector.tensor_copy(b_part[l][rows, :], b_tmp[l][rows, :]).then_inc(b_step, 1)
                    bs += 1
                    if part < BPARTS - 1:
                        nc.vector.tensor_tensor(b_rest[l][:, :], rest[:, :], b_tmp[l][:, :],
                                                ALU.subtract).then_inc(b_step, 1)
                        bs += 1
                        dve.wait_ge(b_step, bs)
                        rest = b_rest[l]
            assert bs == B_STEPS

            for l in L:
                for kind, hi, done in (("x", wx_hi, wx_ready), ("h", wh_hi, wh_ready)):
                    dve.wait_ge(hi[l], 1)
                    nc.vector.scalar_tensor_tensor(
                        out=w_part[kind, l][:, :, LO, :], in0=w_f32[kind, l][:, :, :], scalar=WSCALE,
                        in1=w_part[kind, l][:, :, HI, :], op0=ALU.mult, op1=ALU.subtract).then_inc(done[l], 1)

            registers = [[dve.alloc_register(f"due_{n}_{h}") for h in range(H)] for n in range(2)]

            def counts(n, c, u):
                values = [halves(c, u, h) for h in range(H)]
                if isinstance(c, int):
                    return values
                for register, value in zip(registers[n % 2], values):
                    dve.reg_mov(register, value)
                return [dve.snap(register) for register in registers[n % 2]]

            def steps(order):
                order = list(order)
                due = counts(0, *order[0][1:])
                for n, (l, c, u) in enumerate(order):
                    now = due
                    for h in range(H):
                        dve.wait_ge(z_ready[l], now[h])
                        nc.vector.tensor_reduce(z_sum[l][:, half(h), :],
                                                z_chunk[l][h][:, :, u, :, :].rearrange("p m s b -> p m b s"),
                                                AX.X, ALU.add).then_inc(sum_ready[l], 1)
                    if n + 1 < len(order):
                        due = counts(n + 1, *order[n + 1][1:])
                    for h in range(H):
                        dve.wait_ge(tanh_done[l], now[h])
                        nc.vector.tensor_tensor(h_part[l][:, half(h), LO, :], h_chunk[l][:, half(h), u, :],
                                                h_part[l][:, half(h), HI, :],
                                                ALU.subtract).then_inc(h_ready[l], 1)

            steps((0, 0, u) for u in range(U))
            with dve.Fori(1, C) as c:
                steps((l, c - l, u) for u in range(U) for l in L)
            steps((1, C - 1, u) for u in range(U))

        @block.tensor
        def _(pe):
            def project(l, c):
                pe.wait_ge(x_ready[l], c + 1)
                pe.wait_ge(h_ready[l], c * (H * U) + H)
                for h in range(H):
                    nc.tensor.matmul(z_chunk[l][h][:, :, :, HI, :], b_part[l][:, :], b_select[:, half(h), :, :],
                                     start=True, stop=False, skip_group_check=True)
                    for m in range(MH):
                        mm = h * MH + m
                        for k in range(M):
                            for w in range(S):
                                last = nc.tensor.matmul(
                                    Z[l][h][:, m * U * S * B:(m + 1) * U * S * B],
                                    w_part["x", l][:, k, w, mm * P:(mm + 1) * P],
                                    x_part[l][:, k, :, :, :].rearrange("p u s b -> p (u s b)"),
                                    start=False, stop=False, skip_group_check=True)
                last.then_inc(proj_done[l], 1)

            def step(l, c, u):
                for hk in range(H):
                    for h in range(H):
                        if hk == 0:
                            pe.wait_ge(h_ready[l], halves(c, u, h))
                        for m in range(MH):
                            mm = h * MH + m
                            at = (m * U + u) * S * B
                            for k in range(hk * MH, (hk + 1) * MH):
                                for w in range(S):
                                    last = nc.tensor.matmul(
                                        Z[l][h][:, at:at + NW], w_part["h", l][:, k, w, mm * P:(mm + 1) * P],
                                        h_wide[l][:, k, :], start=False, stop=True, skip_group_check=True)
                        if hk == H - 1:
                            last.then_inc(z_ready[l], 1)

            pe.wait_ge(select_step, 1 + BPARTS)
            pe.wait_ge(b_step, B_STEPS)
            pe.wait_ge(wx_ready[0], 1)
            project(0, 0)
            pe.wait_ge(wh_ready[0], 1)
            for u in range(U):
                step(0, 0, u)
            pe.wait_ge(wx_ready[1], 1)
            pe.wait_ge(wh_ready[1], 1)
            with pe.Fori(1, C) as c:
                project(0, c)
                step(0, c, 0)
                project(1, c - 1)
                step(1, c - 1, 0)
                for u in range(1, U):
                    step(0, c, u)
                    step(1, c - 1, u)
            project(1, C - 1)
            for u in range(U):
                step(1, C - 1, u)


def kernel(x, cond_1024, L0_cond_Wx, L0_cond_Wh, L0_cond_b, L1_cond_Wx, L1_cond_Wh, L1_cond_b):
    import numpy as np
    import concourse.bacc as bacc
    from concourse.bass_utils import run_bass_kernel_spmd

    P, U = 128, 16
    x, cond = np.asarray(x), np.asarray(cond_1024)
    B, T, D = x.shape
    M, C = D // P, T // U
    x_t = x.reshape(B, C, U, M, P).transpose(4, 1, 3, 2, 0).reshape(P, -1)
    cond_t = cond.reshape(B, M, P).transpose(2, 1, 0).reshape(P, -1)
    arrays = {"x_t": x_t, "cond_t": cond_t, "wx0": L0_cond_Wx, "wh0": L0_cond_Wh, "b0": L0_cond_b,
              "wx1": L1_cond_Wx, "wh1": L1_cond_Wh, "b1": L1_cond_b}
    arrays = {name: np.ascontiguousarray(a) for name, a in arrays.items()}

    nc = bacc.Bacc("TRN2", target_bir_lowering=False, num_devices=1)
    ins = [nc.dram_tensor(name, a.shape, mybir.dt.from_np(a.dtype), kind="ExternalInput").ap()
           for name, a in arrays.items()]
    out_t = nc.dram_tensor("out_t", x_t.shape, mybir.dt.float32, kind="ExternalOutput").ap()
    residual_rnn_pair(nc, *ins, out_t)
    r = run_bass_kernel_spmd(nc, [arrays], core_ids=[0])
    got = r.results[0]["out_t"]
    return np.ascontiguousarray(got.reshape(P, C, M, U, B).transpose(4, 1, 3, 2, 0).reshape(B, T, D))
```

```python
import concourse.bass as bass
from concourse import mybir
from contextlib import ExitStack


def residual_rnn_pair(nc, x_t, cond_t, wx0, wh0, b0, wx1, wh1, b1, out_t):
    fp32 = mybir.dt.float32
    fp16 = mybir.dt.float16
    ALU = mybir.AluOpType
    ACT = mybir.ActivationFunctionType
    AX = mybir.AxisListType

    P = 128
    D = wx0.shape[0]
    M = D // P
    B = cond_t.shape[1] // M
    U = 16
    CW = M * U * B
    C = x_t.shape[1] // CW
    S = 2
    HI, LO = 0, 1
    NW = 32
    H = 2
    MH = M // H
    L = (0, 1)
    WSCALE = 4096.0
    BPARTS = 3

    STORES = [32, 32, 32, 16, 8, 4, 2, 1, 1]
    assert sum(STORES) == C
    B_STEPS = 3 * BPARTS - 1

    W_BLOCKS = [(kind, k) for kind in ("x", "h") for k in range(M)]
    assert len(W_BLOCKS) + BPARTS < U

    wx, wh, bias = (wx0, wx1), (wh0, wh1), (b0, b1)

    with ExitStack() as ctx:
        def sb(name, shape, dt):
            return ctx.enter_context(nc.sbuf_tensor(name, shape, dt))

        def sem(name):
            return ctx.enter_context(nc.semaphore(name))

        def per_layer(make, name, *args):
            return [make(f"{name}{l}", *args) for l in L]

        X = sb("X", [P, C * CW], fp32)
        cond = sb("cond", [P, M * B], fp32)
        w_f32 = {(kind, l): sb(f"w_f32_{kind}{l}", [P, M, D], fp32) for l in L for kind in ("x", "h")}
        w_part = {(kind, l): sb(f"w_part_{kind}{l}", [P, M, S, D], fp16) for l in L for kind in ("x", "h")}
        b_f32 = per_layer(sb, "b_f32_", [P, P], fp32)
        b_rest = per_layer(sb, "b_rest_", [P, P], fp32)
        b_tmp = per_layer(sb, "b_tmp_", [P, P], fp16)
        b_part = per_layer(sb, "b_part_", [P, P], fp16)
        b_select = sb("b_select", [P, M, U, B], fp16)
        x_part = per_layer(sb, "x_part_", [P, M, U, S, B], fp16)
        h_wide = per_layer(sb, "h_wide_", [P, M, NW], fp16)
        h_part = [h[:, :, 0:S * B].rearrange("p m (s b) -> p m s b", s=S) for h in h_wide]
        h_chunk = per_layer(sb, "h_chunk_", [P, M, U, B], fp32)
        z_sum = per_layer(sb, "z_sum_", [P, M, B], fp32)
        Z = [[ctx.enter_context(nc.psum_tensor(f"Z{l}_{h}", [P, 512], fp32)) for h in range(H)] for l in L]
        z_chunk = [[z[:, 0:MH * U * S * B].rearrange("p (m u s b) -> p m u s b", m=MH, u=U, s=S) for z in zs]
                   for zs in Z]

        cond_loaded = sem("cond_loaded")
        x_first_loaded = sem("x_first_loaded")
        x_rest_loaded = sem("x_rest_loaded")
        b_loaded = per_layer(sem, "b_loaded_")
        wx_loaded = [[sem(f"wx_loaded_{l}_{h}") for h in range(H)] for l in L]
        wh_loaded = [[sem(f"wh_loaded_{l}_{h}") for h in range(H)] for l in L]
        zeroed = sem("zeroed")
        select_step = sem("select_step")
        wx_hi = per_layer(sem, "wx_hi_")
        wh_hi = per_layer(sem, "wh_hi_")
        wx_ready = per_layer(sem, "wx_ready_")
        wh_ready = per_layer(sem, "wh_ready_")
        b_step = sem("b_step")
        h0_hi = sem("h0_hi")
        x_hi = per_layer(sem, "x_hi_")
        x_ready = sem("x_ready")
        proj_done = per_layer(sem, "proj_done_")
        z_ready = per_layer(sem, "z_ready_")
        sum_ready = per_layer(sem, "sum_ready_")
        tanh_done = per_layer(sem, "tanh_done_")
        h_ready = per_layer(sem, "h_ready_")
        h_used = per_layer(sem, "h_used_")
        pool_waited = sem("pool_waited")
        stored = sem("stored")

        def half(h):
            return slice(h * MH, (h + 1) * MH)

        def halves(c, u, h):
            return c * (H * U) + (H * u + h + 1)

        def x_splits(l, c):
            if isinstance(c, int) and (l, c) == (0, 0):
                return 1
            return 2 * c + (0, 3)[l]

        block = ctx.enter_context(nc.Block())
        FIRST = 2 * CW

        @block.sync
        def _(sp):
            def load_weights(kind, l, w, loaded):
                for h in range(H):
                    sp.dma_start(w_f32[kind, l][:, half(h), :],
                                 w[l].rearrange("(k p) n -> p k n", p=P)[:, half(h), :]).then_inc(loaded[l][h], 16)

            def load_bias(l):
                for part in range(BPARTS):
                    sp.dma_start(b_f32[l][32 * part:32 * part + M, :],
                                 bias[l].rearrange("(m p) -> m p", p=P)).then_inc(b_loaded[l], 16)

            load_weights("x", 0, wx, wx_loaded)
            sp.dma_start(X[:, 0:FIRST], x_t[:, 0:FIRST]).then_inc(x_first_loaded, 16)
            sp.wait_ge(zeroed, 1)
            load_bias(0)
            sp.dma_start(cond[:, :], cond_t).then_inc(cond_loaded, 16)
            load_weights("h", 0, wh, wh_loaded)
            load_bias(1)
            load_weights("x", 1, wx, wx_loaded)
            load_weights("h", 1, wh, wh_loaded)
            sp.dma_start(X[:, FIRST:], x_t[:, FIRST:]).then_inc(x_rest_loaded, 16)
            c = 0
            for n in STORES:
                sp.wait_ge(h_used[1], 1 + c + n)
                sp.dma_start(out_t[:, c * CW:(c + n) * CW], X[:, c * CW:(c + n) * CW]).then_inc(stored, 16)
                c += n
            sp.wait_ge(stored, 16 * len(STORES))

        @block.gpsimd
        def _(pool):
            nc.gpsimd.memset(b_select[:, :, :, :], 0.0).then_inc(select_step, 1)
            for part in range(BPARTS):
                pool.wait_ge(select_step, part + 1)
                nc.gpsimd.affine_select(out=b_select[:, :, :, :], in_=b_select[:, :, :, :], compare_op=ALU.not_equal,
                                        fill=WSCALE, base=-32 * part, pattern=[[-1, M], [0, U], [0, B]],
                                        channel_multiplier=1).then_inc(select_step, 1)

            def chunk(c):
                return X[:, bass.ds(c * CW, CW)].rearrange("p (m u b) -> p m u b", m=M, u=U)

            def wait_apart(what, value):
                pool.wait_ge(what, value)
                pool.sem_inc(pool_waited, 1)

            def split_lo(l, c):
                wait_apart(x_hi[l], c + 1)
                nc.gpsimd.tensor_tensor(x_part[l][:, :, :, LO, :], chunk(c), x_part[l][:, :, :, HI, :],
                                        ALU.subtract).then_inc(x_ready, 1)

            def split_x0(c):
                nc.gpsimd.tensor_copy(x_part[0][:, :, :, HI, :], chunk(c)).then_inc(x_hi[0], 1)
                split_lo(0, c)

            def add_states(l, c):
                nc.gpsimd.tensor_tensor(chunk(c), chunk(c), h_chunk[l][:, :, :, :], ALU.add).then_inc(h_used[l], 1)

            def turn(c, split0=True, layer0=True, layer1=True):
                if split0:
                    wait_apart(proj_done[0], c + 1)
                    split_x0(c + 1)
                if layer0:
                    if not isinstance(c, int) or c >= 1:
                        wait_apart(proj_done[1], c)
                    wait_apart(tanh_done[0], c * (H * U) + H * U)
                    nc.gpsimd.tensor_tensor(x_part[1][:, :, :, HI, :], chunk(c), h_chunk[0][:, :, :, :],
                                            ALU.add).then_inc(x_hi[1], 1)
                    add_states(0, c)
                    wait_apart(h_used[0], 1 + c + 1)
                    split_lo(1, c)
                if layer1:
                    wait_apart(tanh_done[1], c * (H * U))
                    add_states(1, c - 1)

            for l in L:
                pool.sem_inc(h_used[l], 1)
            pool.wait_ge(x_first_loaded, 16)
            split_x0(0)

            pool.wait_ge(cond_loaded, 16)
            pool.wait_ge(zeroed, 1)
            start = cond[:, :].rearrange("p (m b) -> p m b", m=M)
            for l in L:
                nc.gpsimd.tensor_copy(h_part[l][:, :, HI, :], start).then_inc(h0_hi, 1)
            for l in L:
                pool.wait_ge(h0_hi, l + 1)
                for h in range(H):
                    nc.gpsimd.tensor_tensor(h_part[l][:, half(h), LO, :], start[:, half(h), :],
                                            h_part[l][:, half(h), HI, :], ALU.subtract).then_inc(h_ready[l], 1)

            turn(0, layer1=False)
            pool.wait_ge(x_rest_loaded, 16)
            with pool.Fori(1, C - 1) as c:
                turn(c)
            turn(C - 1, split0=False)
            turn(C, split0=False, layer0=False)

        @block.scalar
        def _(act):
            def convert_weights(l, kind, k):
                loaded, done = (wx_loaded, wx_hi) if kind == "x" else (wh_loaded, wh_hi)
                if k % MH == 0:
                    act.wait_ge(loaded[l][k // MH], 16)
                nc.scalar.activation(w_part[kind, l][:, k, HI, :], w_f32[kind, l][:, k, :], ACT.Copy,
                                     scale=WSCALE).then_inc(done[l], 1)

            for kind, k in W_BLOCKS:
                convert_weights(0, kind, k)

            def step(l, c, u):
                if u == 0:
                    act.wait_ge(h_used[l], 1 + c)
                for h in range(H):
                    act.wait_ge(sum_ready[l], halves(c, u, h))
                    nc.scalar.activation(h_part[l][:, half(h), HI, :], z_sum[l][:, half(h), :], ACT.Tanh,
                                         scale=1.0 / WSCALE)
                    nc.scalar.activation(h_chunk[l][:, half(h), u, :], z_sum[l][:, half(h), :], ACT.Tanh,
                                         scale=1.0 / WSCALE).then_inc(tanh_done[l], 1)

            for u in range(U):
                step(0, 0, u)
                if u < len(W_BLOCKS):
                    convert_weights(1, *W_BLOCKS[u])
            with act.Fori(1, C) as c:
                for u in range(U):
                    step(0, c, u)
                    step(1, c - 1, u)
            for u in range(U):
                step(1, C - 1, u)

        @block.vector
        def _(dve):
            for l in L:
                nc.vector.memset(b_f32[l][:, :], 0.0)
                nc.vector.memset(b_part[l][:, :], 0.0)
                last = nc.vector.memset(h_wide[l][:, :, :], 0.0)
            last.then_inc(zeroed, 1)

            def split_bias(l, part):
                step = l * B_STEPS + 3 * part
                if part == 0:
                    dve.wait_ge(b_loaded[l], 16 * BPARTS)
                rest = b_rest[l] if part else b_f32[l]
                if part:
                    dve.wait_ge(b_step, step)
                nc.vector.tensor_copy(b_tmp[l][:, :], rest[:, :]).then_inc(b_step, 1)
                dve.wait_ge(b_step, step + 1)
                rows = slice(32 * part, 32 * part + M)
                nc.vector.tensor_copy(b_part[l][rows, :], b_tmp[l][rows, :]).then_inc(b_step, 1)
                if part < BPARTS - 1:
                    nc.vector.tensor_tensor(b_rest[l][:, :], rest[:, :], b_tmp[l][:, :],
                                            ALU.subtract).then_inc(b_step, 1)

            def split_weights(l, kind, k):
                hi, done = (wx_hi, wx_ready) if kind == "x" else (wh_hi, wh_ready)
                dve.wait_ge(hi[l], k + 1)
                nc.vector.scalar_tensor_tensor(
                    out=w_part[kind, l][:, k, LO, :], in0=w_f32[kind, l][:, k, :], scalar=WSCALE,
                    in1=w_part[kind, l][:, k, HI, :], op0=ALU.mult, op1=ALU.subtract).then_inc(done[l], 1)

            for kind, k in W_BLOCKS[:M]:
                split_weights(0, kind, k)
            for part in range(BPARTS):
                split_bias(0, part)
            for kind, k in W_BLOCKS[M:]:
                split_weights(0, kind, k)

            def split_layer1(u):
                if 1 <= u <= len(W_BLOCKS):
                    split_weights(1, *W_BLOCKS[u - 1])
                if 0 < u - len(W_BLOCKS) <= BPARTS:
                    split_bias(1, u - len(W_BLOCKS) - 1)

            registers = [[dve.alloc_register(f"due_{n}_{h}") for h in range(H)] for n in range(2)]

            def counts(n, c, u):
                values = [halves(c, u, h) for h in range(H)]
                if isinstance(c, int):
                    return values
                for register, value in zip(registers[n % 2], values):
                    dve.reg_mov(register, value)
                return [dve.snap(register) for register in registers[n % 2]]

            def steps(order, behind=None):
                order = list(order)
                due = counts(0, *order[0][1:])
                for n, (l, c, u) in enumerate(order):
                    now = due
                    for h in range(H):
                        dve.wait_ge(z_ready[l], now[h])
                        nc.vector.tensor_reduce(z_sum[l][:, half(h), :],
                                                z_chunk[l][h][:, :, u, :, :].rearrange("p m s b -> p m b s"),
                                                AX.X, ALU.add).then_inc(sum_ready[l], 1)
                    if n + 1 < len(order):
                        due = counts(n + 1, *order[n + 1][1:])
                    for h in range(H):
                        dve.wait_ge(tanh_done[l], now[h])
                        nc.vector.tensor_tensor(h_part[l][:, half(h), LO, :], h_chunk[l][:, half(h), u, :],
                                                h_part[l][:, half(h), HI, :],
                                                ALU.subtract).then_inc(h_ready[l], 1)
                    if behind:
                        behind(u)

            steps(((0, 0, u) for u in range(U)), behind=split_layer1)
            with dve.Fori(1, C) as c:
                steps((l, c - l, u) for u in range(U) for l in L)
            steps((1, C - 1, u) for u in range(U))

        @block.tensor
        def _(pe):
            def project(l, c):
                for h in range(H):
                    nc.tensor.matmul(z_chunk[l][h][:, :, :, HI, :], b_part[l][:, :], b_select[:, half(h), :, :],
                                     start=True, stop=False, skip_group_check=True)
                    for m in range(MH):
                        mm = h * MH + m
                        for k in range(M):
                            for w in range(S):
                                last = nc.tensor.matmul(
                                    Z[l][h][:, m * U * S * B:(m + 1) * U * S * B],
                                    w_part["x", l][:, k, w, mm * P:(mm + 1) * P],
                                    x_part[l][:, k, :, :, :].rearrange("p u s b -> p (u s b)"),
                                    start=False, stop=False, skip_group_check=True)
                last.then_inc(proj_done[l], 1)

            def step(l, c, u, before_second=None):
                for hk in range(H):
                    for h in range(H):
                        if hk == 0:
                            pe.wait_ge(h_ready[l], halves(c, u, h))
                        for m in range(MH):
                            mm = h * MH + m
                            at = (m * U + u) * S * B
                            if hk == H - 1 and mm == 0 and before_second:
                                before_second()
                            for k in range(hk * MH, (hk + 1) * MH):
                                for w in range(S):
                                    last = nc.tensor.matmul(
                                        Z[l][h][:, at:at + NW], w_part["h", l][:, k, w, mm * P:(mm + 1) * P],
                                        h_wide[l][:, k, :], start=False, stop=True, skip_group_check=True)
                        if hk == H - 1:
                            last.then_inc(z_ready[l], 1)

            TURNS = 3
            PEELED = 1 + (C - 1) // TURNS * TURNS

            pe.wait_ge(select_step, 1 + BPARTS)
            pe.wait_ge(b_step, B_STEPS)
            pe.wait_ge(wx_ready[0], M)
            pe.wait_ge(x_ready, x_splits(0, 0))
            project(0, 0)
            pe.wait_ge(wh_ready[0], M)
            for u in range(U):
                step(0, 0, u)
            pe.wait_ge(b_step, 2 * B_STEPS)
            pe.wait_ge(wx_ready[1], M)
            pe.wait_ge(wh_ready[1], M)
            pe.wait_ge(x_ready, x_splits(0, 1))
            pe.wait_ge(sum_ready[0], H * U)

            def turn(c, last=False):
                project(0, c)
                step(0, c, 0)
                pe.wait_ge(x_ready, x_splits(1, c - 1))
                pe.wait_ge(h_ready[1], (c - 1) * (H * U) + H)
                project(1, c - 1)
                step(1, c - 1, 0)
                for u in range(1, U - 1):
                    step(0, c, u)
                    step(1, c - 1, u)
                step(0, c, U - 1)

                def await_next():
                    pe.wait_ge(x_ready, x_splits(0, c + 1))
                    pe.wait_ge(sum_ready[0], (c + 1) * (H * U))

                step(1, c - 1, U - 1, before_second=None if last else await_next)

            with nc.Fori(1, PEELED, TURNS, engines=(mybir.EngineType.PE,), hint_back_edge=True) as c:
                for n in range(TURNS):
                    turn(c + n)
            for c in range(PEELED, C):
                turn(c, last=c == C - 1)
            pe.wait_ge(x_ready, x_splits(1, C - 1) - 1)
            pe.wait_ge(h_ready[1], (C - 1) * (H * U) + H)
            project(1, C - 1)
            for u in range(U):
                step(1, C - 1, u)


def kernel(x, cond_1024, L0_cond_Wx, L0_cond_Wh, L0_cond_b, L1_cond_Wx, L1_cond_Wh, L1_cond_b):
    import numpy as np
    import concourse.bacc as bacc
    from concourse.bass_utils import run_bass_kernel_spmd

    P, U = 128, 16
    x, cond = np.asarray(x), np.asarray(cond_1024)
    B, T, D = x.shape
    M, C = D // P, T // U
    x_t = x.reshape(B, C, U, M, P).transpose(4, 1, 3, 2, 0).reshape(P, -1)
    cond_t = cond.reshape(B, M, P).transpose(2, 1, 0).reshape(P, -1)
    arrays = {"x_t": x_t, "cond_t": cond_t, "wx0": L0_cond_Wx, "wh0": L0_cond_Wh, "b0": L0_cond_b,
              "wx1": L1_cond_Wx, "wh1": L1_cond_Wh, "b1": L1_cond_b}
    arrays = {name: np.ascontiguousarray(a) for name, a in arrays.items()}

    nc = bacc.Bacc("TRN2", target_bir_lowering=False, num_devices=1)
    ins = [nc.dram_tensor(name, a.shape, mybir.dt.from_np(a.dtype), kind="ExternalInput").ap()
           for name, a in arrays.items()]
    out_t = nc.dram_tensor("out_t", x_t.shape, mybir.dt.float32, kind="ExternalOutput").ap()
    residual_rnn_pair(nc, *ins, out_t)
    r = run_bass_kernel_spmd(nc, [arrays], core_ids=[0])
    got = r.results[0]["out_t"]
    return np.ascontiguousarray(got.reshape(P, C, M, U, B).transpose(4, 1, 3, 2, 0).reshape(B, T, D))
```
